# Optimizing a Trainium2 kernel written in Bass

```python
import numpy as np
import jax
import jax.numpy as jnp

def _softmax(x, axis=-1):
    return jax.nn.softmax(x, axis=axis)

def _gelu(x):
    return jax.nn.gelu(x, approximate=True)

def _silu(x):
    return jax.nn.silu(x)

def _sigmoid(x):
    return jax.nn.sigmoid(x)

def _layernorm(x, axis=-1, eps=1e-05):
    m = jnp.mean(x, axis=axis, keepdims=True)
    v = jnp.var(x, axis=axis, keepdims=True)
    return (x - m) / jnp.sqrt(v + eps)

def _scatter_add(tgt, idx, src, axis=0):
    return tgt.at[idx].add(src)

def _segment_sum(src, seg, n):
    return jax.ops.segment_sum(src, seg, n)
kernel_name = 'mk_seq_postln_d1_jaxref_r4_e1000f'

def setup_inputs(seed: int=0):
    np.random.seed(seed)
    _w = jnp.asarray

    def _L0_attn_setup():
        import math
        import jax, jax.numpy as jnp
        import numpy as np

        def _rope_tables(T, h, dtype):
            pos = jnp.arange(T, dtype=jnp.float32)
            thetas = 1.0 / 10000.0 ** (jnp.arange(0, h, 2, dtype=jnp.float32) / h)
            pt = jnp.outer(pos, thetas)
            pt = jnp.concatenate([pt, pt], axis=-1)
            return (jnp.sin(pt).astype(dtype), jnp.cos(pt).astype(dtype))

        def _apply_rope(x, sin, cos):
            h = x.shape[-1]
            rot = jnp.concatenate([-x[..., h // 2:], x[..., :h // 2]], axis=-1)
            return x * cos + rot * sin
        key = jax.random.key(seed)
        ks = jax.random.split(key, 5)
        B, T, C = (2, 512, 1024)
        s = 1.0 / math.sqrt(C)
        return {'x': jax.random.normal(ks[0], (B, T, C), dtype=jnp.float32), 'wq': jax.random.normal(ks[1], (C, C), dtype=jnp.float32) * s, 'wk': jax.random.normal(ks[2], (C, C), dtype=jnp.float32) * s, 'wv': jax.random.normal(ks[3], (C, C), dtype=jnp.float32) * s, 'wo': jax.random.normal(ks[4], (C, C), dtype=jnp.float32) * s}
    _L0_attn_in = _L0_attn_setup()

    def _L0_ffn_setup():
        import jax, jax.numpy as jnp
        import numpy as np
        H = 1024
        I = 2752
        CS = 8
        CB = 16384

        def _dequant(codebook, idx):
            return codebook[idx].reshape(idx.shape[0], -1)
        key = jax.random.key(seed)
        k0, k1, k2, k3, k4 = jax.random.split(key, 5)
        x = jax.random.normal(k0, (4, 512, H), dtype=jnp.float32)
        codebook = jax.random.normal(k1, (CB, CS), dtype=jnp.float32)
        idx_gate = jax.random.randint(k2, (I, H // CS), 0, CB, dtype=jnp.int32)
        idx_up = jax.random.randint(k3, (I, H // CS), 0, CB, dtype=jnp.int32)
        idx_down = jax.random.randint(k4, (H, I // CS), 0, CB, dtype=jnp.int32)
        return {'x': x, 'codebook': codebook, 'idx_gate': idx_gate, 'idx_up': idx_up, 'idx_down': idx_down}
    _L0_ffn_in = _L0_ffn_setup()
    _d = {'L0_attn_x': _L0_attn_in['x'], 'L0_attn_wq': _L0_attn_in['wq'], 'L0_attn_wk': _L0_attn_in['wk'], 'L0_attn_wv': _L0_attn_in['wv'], 'L0_attn_wo': _L0_attn_in['wo'], 'L0_ffn_codebook': _L0_ffn_in['codebook'], 'L0_ffn_idx_gate': _L0_ffn_in['idx_gate'], 'L0_ffn_idx_up': _L0_ffn_in['idx_up'], 'L0_ffn_idx_down': _L0_ffn_in['idx_down']}
    _x0 = _d['L0_attn_x']
    _d['L0_attn_x'] = jax.random.normal(jax.random.fold_in(jax.random.key(seed), 1), (2, 1024, 1024), dtype=_x0.dtype)
    del _x0
    return _d

def reference(L0_attn_x, L0_attn_wq, L0_attn_wk, L0_attn_wv, L0_attn_wo, L0_ffn_codebook, L0_ffn_idx_gate, L0_ffn_idx_up, L0_ffn_idx_down):

    def _L0_attn_ref(x, wq, wk, wv, wo):
        import math
        import jax, jax.numpy as jnp
        import numpy as np

        def _rope_tables(T, h, dtype):
            pos = jnp.arange(T, dtype=jnp.float32)
            thetas = 1.0 / 10000.0 ** (jnp.arange(0, h, 2, dtype=jnp.float32) / h)
            pt = jnp.outer(pos, thetas)
            pt = jnp.concatenate([pt, pt], axis=-1)
            return (jnp.sin(pt).astype(dtype), jnp.cos(pt).astype(dtype))

        def _apply_rope(x, sin, cos):
            h = x.shape[-1]
            rot = jnp.concatenate([-x[..., h // 2:], x[..., :h // 2]], axis=-1)
            return x * cos + rot * sin
        B, T, C = x.shape
        n_head = 32
        h = C // n_head

        def proj(w):
            y = jnp.einsum('btc,dc->btd', x, w)
            return y.reshape(B, T, n_head, h).transpose(0, 2, 1, 3)
        q, k, v = (proj(wq), proj(wk), proj(wv))
        sin, cos = _rope_tables(T, h, x.dtype)
        q = _apply_rope(q, sin, cos)
        k = _apply_rope(k, sin, cos)
        scores = jnp.einsum('bnth,bnsh->bnts', q, k) * (1.0 / math.sqrt(h))
        causal = jnp.tril(jnp.ones((T, T), dtype=bool))
        scores = jnp.where(causal, scores, -jnp.inf)
        attn = jax.nn.softmax(scores, axis=-1)
        out = jnp.einsum('bnts,bnsh->bnth', attn, v)
        out = out.transpose(0, 2, 1, 3).reshape(B, T, C)
        return jnp.einsum('btc,dc->btd', out, wo)

    def _L0_ffn_ref(x, codebook, idx_gate, idx_up, idx_down):
        import jax, jax.numpy as jnp
        import numpy as np
        H = 1024
        I = 2752
        CS = 8
        CB = 16384

        def _dequant(codebook, idx):
            return codebook[idx].reshape(idx.shape[0], -1)
        Wg = _dequant(codebook, idx_gate)
        Wu = _dequant(codebook, idx_up)
        Wd = _dequant(codebook, idx_down)
        g = jnp.einsum('bsh,ih->bsi', x, Wg)
        u = jnp.einsum('bsh,ih->bsi', x, Wu)
        h = jax.nn.silu(g) * u
        return jnp.einsum('bsi,hi->bsh', h, Wd)
    x = L0_attn_x
    x = _layernorm(x + _L0_attn_ref(x, L0_attn_wq, L0_attn_wk, L0_attn_wv, L0_attn_wo), axis=-1)
    x = _layernorm(x + _L0_ffn_ref(x, L0_ffn_codebook, L0_ffn_idx_gate, L0_ffn_idx_up, L0_ffn_idx_down), axis=-1)
    return x

_drawn_inputs = setup_inputs


def setup_inputs(seed=0):
    import zlib

    import numpy as np

    out = dict(_drawn_inputs(seed))
    spreads = {}
    factors = {}
    for name, (base, spread) in spreads.items():
        noise = np.random.default_rng([zlib.crc32(name.encode()), seed]).standard_normal(out[name].shape)
        drawn = base * np.exp(spread * noise) if base else spread * noise
        out[name] = jnp.asarray(drawn.astype(out[name].dtype))
    for name, factor in factors.items():
        out[name] = (out[name] * factor).astype(out[name].dtype)
    return out
```

```python
from contextlib import ExitStack

import numpy as np

import concourse.bass as bass
import concourse.mybir as mybir

ACT = mybir.ActivationFunctionType
ALU = mybir.AluOpType
AX = mybir.AxisListType
F32 = mybir.dt.float32
BF16 = mybir.dt.bfloat16
I32 = mybir.dt.int32

P = 128
B, T, C = 2, 1024, 1024
S = B * T
NHEAD = 32
HD = C // NHEAD
SCALE = 1.0 / HD ** 0.5
HG = P // HD
KT = C // P
NG = C // P
TB = T // P
SB = S // P
INNER = 2752
CS = 8
NJ = INNER // CS
JBLOCKS = [(j0, min(P, NJ - j0)) for j0 in range(0, NJ, P)]
PAIRS = CS + CS // 2
NPAIR = PAIRS * len(JBLOCKS)
N = 512
NT = S // N
EPS = 1e-5
MASKED = -1e30
STEPS = HG * TB


def seq_post_ln_layer(nc, x_nat, xT, wqT, wkT, wvT, woT, codebook, idx, cos, sin, rot, ident, mask, out):
    ctx = ExitStack()
    with ctx:
        sb = lambda name, shape, dt: ctx.enter_context(nc.sbuf_tensor(name, shape, dt))
        sem = lambda name: ctx.enter_context(nc.semaphore(name))

        units = nc.dram_tensor("gathered_units", (NPAIR, 2, P, P * CS), F32)
        yT_dram = nc.dram_tensor("y_partial", (CS, P, S), F32)

        big1 = sb("big1", [P, CS, S], F32)
        big2 = sb("big2", [P, CS, S], F32)
        raw = sb("raw", [P, 2, P, CS], F32)
        idx_sb = sb("idx_sb", [P, 2, P], I32)
        id_sb = sb("id_sb", [P, P], F32)
        rot_sb = sb("rot_sb", [P, P], F32)
        mask_sb = sb("mask_sb", [P, P], BF16)
        idb_sb = sb("idb_sb", [P, P], BF16)
        small = sb("small", [P, 64], F32)
        arena = sb("arena", [P, 60 * 256], F32)
        ps = ctx.enter_context(nc.psum_tensor("ps", [P, 8, N], F32))

        kb = lambda a, n: arena[:, a * 256:(a + n) * 256]
        w_sb = kb(0, 12).rearrange("p (m k d) -> p m k d", m=3, k=KT)
        qkv = kb(12, 12).rearrange("p (m t) -> p m t", m=3)
        rtmp = kb(24, 8).rearrange("p (m t) -> p m t", m=2)
        v_nat = kb(32, 4).rearrange("p (s d) -> p s d", s=TB)
        probs = kb(36, 8).rearrange("p (b s) -> p b s", b=2)
        probsT = kb(44, 8).rearrange("p (b s t) -> p b s t", b=2, s=TB)
        cos_sb, sin_sb = kb(52, 4), kb(56, 4)
        wo_sb = kb(0, 32).rearrange("p (g d) -> p g d", g=NG)
        o_blk = kb(32, 4).rearrange("p (g s) -> p g s", g=NG)
        x_blk, x1_blk = kb(36, 4), kb(40, 4)
        w_raw = kb(0, 8).rearrange("p (b n e) -> p b n e", b=2, e=CS)
        w_rep = kb(8, 8).rearrange("p (b e n) -> p b e n", b=2, e=CS)
        silu = kb(16, 4).rearrange("p (b s) -> p b s", b=2)
        y_sb = kb(20, 16).rearrange("p (b s) -> p b s", b=2)
        y_blk = kb(36, 4).rearrange("p (e s) -> p e s", e=CS)
        out_blk = kb(40, 4)
        rowmax, negmax, rowsum, rinv = small[:, 0:2], small[:, 2:4], small[:, 4:6], small[:, 6:8]
        stats = small[:, 8:20].rearrange("p (n k) -> p n k", n=2)
        meanvar, std, rstd, eps_sb = small[:, 20:22], small[:, 22:23], small[:, 23:24], small[:, 24:25]

        pool_passed = sem("pool_passed"); dve_passed = sem("dve_passed"); pe_passed = sem("pe_passed")
        idx_in = [sem(f"idx_in{s}") for s in range(2)]
        gathered = [[sem(f"gathered{jb}_{s}") for s in range(2)] for jb in range(len(JBLOCKS))]
        stored = [sem(f"stored{s}") for s in range(2)]
        const_in = sem("const_in"); mask_ready = sem("mask_ready"); xT_in = sem("xT_in"); w_in = sem("w_in")
        proj_done = sem("proj_done"); qkv_copied = sem("qkv_copied"); rot_done = sem("rot_done")
        rope_step = sem("rope_step"); qk_ready = sem("qk_ready")
        vT_done = sem("vT_done"); v_ready = sem("v_ready")
        scores_done = sem("scores_done"); max_done = sem("max_done"); negmax_done = sem("negmax_done")
        exp_done = sem("exp_done"); rinv_done = sem("rinv_done"); probs_ready = sem("probs_ready")
        probsT_done = sem("probsT_done"); probsT_copied = sem("probsT_copied")
        pv_done = sem("pv_done"); oT_ready = sem("oT_ready")
        wo_in = sem("wo_in"); x_in = sem("x_in"); o_blk_ready = sem("o_blk_ready")
        wo_done = sem("wo_done"); sum_ready = sem("sum_ready"); ln_step = sem("ln_step"); var_ready = sem("var_ready")
        std_ready = sem("std_ready"); x1_ready = sem("x1_ready")
        x1T_done = sem("x1T_done"); x1T_ready = sem("x1T_ready"); eps_ready = sem("eps_ready")
        w_loaded = [sem(f"w_loaded{s}") for s in range(2)]
        w_ready = [sem(f"w_ready{s}") for s in range(2)]
        pair_done = [sem(f"pair_done{s}") for s in range(2)]
        gate_done = sem("gate_done"); up_done = sem("up_done")
        silu_ready = sem("silu_ready"); hT_ready = sem("hT_ready")
        down_done = sem("down_done"); y_in = [sem(f"y_in{s}") for s in range(2)]
        y_added = sem("y_added"); y_out = [sem(f"y_out{s}") for s in range(2)]
        y_blk_ready = sem("y_blk_ready"); y_nat_done = sem("y_nat_done")
        var2_ready = sem("var2_ready"); std2_ready = sem("std2_ready"); ln2_step = sem("ln2_step")
        out_ready = sem("out_ready"); out_stored = sem("out_stored")

        block = ctx.enter_context(nc.Block())

        def rows_cols(jb, down):
            nj = JBLOCKS[jb][1]
            return (nj, P) if down else (P, nj)

        @block.gpsimd
        def _(pool):
            def gather_pair(jb, down, pair, first=False):
                rows, cols = rows_cols(jb, down)
                for s in range(2):
                    pool.wait_ge(idx_in[s], 16 * (pair + 1))
                    if not first:
                        pool.wait_ge(stored[s], 16 * pair)
                    pool.sem_inc(pool_passed, 1)
                    for n in range(cols):
                        pool.indirect_dma_start(
                            raw[0:rows, s, n, :], None, codebook,
                            bass.IndirectOffsetOnAxis(ap=idx_sb[0:rows, s, n:n + 1], axis=0),
                        ).then_inc(gathered[jb][s], 16)

            for jb in range(len(JBLOCKS)):
                base = jb * PAIRS
                if jb == 0:
                    gather_pair(jb, False, 0, first=True)
                with pool.Fori(1 if jb == 0 else 0, CS) as e:
                    gather_pair(jb, False, e + base)
                with pool.Fori(0, CS // 2) as k:
                    gather_pair(jb, True, k + (base + CS))

        @block.sync
        def _(sp):
            def load_indices(s, pair):
                sp.dma_start(idx_sb[:, s, :], idx[pair, s]).then_inc(idx_in[s], 16)

            def store_pair(jb, down, pair, count, last=False):
                rows, cols = rows_cols(jb, down)
                for s in range(2):
                    sp.wait_ge(gathered[jb][s], count)
                    sp.dma_start(units[pair, s, 0:rows, 0:cols * CS],
                                 raw[0:rows, s, 0:cols, :].rearrange("p n e -> p (n e)")).then_inc(stored[s], 16)
                    if not last:
                        load_indices(s, pair + 1)

            for s in range(2):
                load_indices(s, 0)
            for jb, (_, nj) in enumerate(JBLOCKS):
                base = jb * PAIRS
                with sp.Fori(0, CS) as e:
                    store_pair(jb, False, e + base, (e + 1) * (16 * nj))
                whole = CS * 16 * nj
                last = jb == len(JBLOCKS) - 1
                with sp.Fori(0, CS // 2 - last) as k:
                    store_pair(jb, True, k + (base + CS), (k + 1) * (16 * P) + whole)
                if last:
                    store_pair(jb, True, NPAIR - 1, CS // 2 * 16 * P + whole, last=True)

        @block.tensor
        def _(pe):
            mm = nc.tensor.matmul

            def attention(i, b):
                for m in range(3):
                    for h in range(2):
                        for k in range(KT):
                            last = mm(ps[:, 2 * m + h, :], w_sb[:, m, k, :],
                                      big1[:, k, bass.ds(b * T + h * N, N)], start=(k == 0), stop=(k == KT - 1))
                    last.then_inc(proj_done, 1)
                for m in range(2):
                    pe.wait_ge(qkv_copied, i * 3 + (m + 1))
                    for h in range(2):
                        last = mm(ps[:, (6 if m == 0 else 0) + h, :], rot_sb[:, :],
                                  qkv[:, m, h * N:(h + 1) * N], start=True, stop=True)
                    last.then_inc(rot_done, 1)
                pe.wait_ge(qkv_copied, i * 3 + 3)
                for s in range(TB):
                    last = nc.tensor.transpose(ps[:, 2 + s // 4, (s % 4) * P:(s % 4 + 1) * P],
                                               qkv[:, 2, s * P:(s + 1) * P], id_sb[:, :])
                last.then_inc(vT_done, 1)

                pe.wait_ge(qk_ready, i * 2 + 2)
                pe.wait_ge(v_ready, i + 1)

                def scores(n):
                    hh, tb = divmod(n, TB)
                    bank, L, r = 4 * (n % 2), (tb + 1) * P, slice(hh * HD, (hh + 1) * HD)
                    if n >= 2:
                        pe.wait_ge(exp_done, i * STEPS + (n - 1))
                    for c0 in range(0, L, N):
                        w = min(N, L - c0)
                        diag = c0 + w == L
                        mm(ps[:, bank + c0 // N, 0:w], qkv[r, 0, tb * P:L], qkv[r, 1, c0:c0 + w],
                           start=True, stop=not diag)
                    d0 = tb * P
                    mm(ps[:, bank + d0 // N, d0 % N:d0 % N + P], idb_sb[:, :], mask_sb[:, :],
                       start=False, stop=True).then_inc(scores_done, 1)

                def turn(n):
                    tb = n % TB
                    pe.wait_ge(probs_ready, i * STEPS + (n + 1))
                    if n >= 1:
                        pe.wait_ge(probsT_copied, i * STEPS + n)
                    for s in range(tb + 1):
                        last = nc.tensor.transpose(ps[:, 2 + s // 4, (s % 4) * P:(s % 4 + 1) * P],
                                                   probs[:, n % 2, s * P:(s + 1) * P], id_sb[:, :])
                    last.then_inc(probsT_done, 1)

                def weigh(n):
                    hh, tb = divmod(n, TB)
                    pe.wait_ge(probsT_copied, i * STEPS + (n + 1))
                    for s in range(tb + 1):
                        last = mm(ps[hh * HD:(hh + 1) * HD, 6 + tb // 4, (tb % 4) * P:(tb % 4 + 1) * P],
                                  v_nat[:, s, hh * HD:(hh + 1) * HD], probsT[:, n % 2, s, :],
                                  start=(s == 0), stop=(s == tb))
                    last.then_inc(pv_done, 1)

                for n in range(STEPS + 2):
                    if n < STEPS:
                        scores(n)
                    if 1 <= n <= STEPS:
                        turn(n - 1)
                    if n >= 2:
                        weigh(n - 2)
                pe.wait_ge(oT_ready, i + 1)

            pe.wait_ge(const_in, 16 * 5)
            pe.wait_ge(xT_in, 16 * KT)
            pe.wait_ge(mask_ready, 2)
            with pe.Fori(0, NG) as g:
                pe.wait_ge(w_in, g * 48 + 48)
                pe.sem_inc(pe_passed, 1)
                with pe.Fori(0, B) as b:
                    attention(g * B + b, b)

            pe.wait_ge(wo_in, 16)
            with pe.Fori(0, SB) as k:
                pe.wait_ge(o_blk_ready, k + 1)
                for h in range(2):
                    for g in range(NG):
                        last = mm(ps[:, h, :], o_blk[:, g, :], wo_sb[:, g, h * N:(h + 1) * N],
                                  start=(g == 0), stop=(g == NG - 1))
                last.then_inc(wo_done, 1)
                pe.wait_ge(x1_ready, k + 1)
                x1_v = x1_blk.rearrange("p (c e) -> p e c", e=CS)
                for e in range(CS):
                    last = nc.tensor.transpose(ps[:, 2 + e // 4, (e % 4) * P:(e % 4 + 1) * P],
                                               x1_v[:, e, :], id_sb[:, :])
                last.then_inc(x1T_done, 1)
                pe.wait_ge(x1T_ready, k + 1)

            def gate_up(nj, jb, e):
                pair, count = e + jb * PAIRS, e + jb * CS
                for s in range(2):
                    pe.wait_ge(w_ready[s], pair + 1)
                for t in range(NT):
                    for s in range(2):
                        for k in range(CS):
                            last = mm(ps[0:nj, 4 * s + t, :], w_rep[:, s, k, 0:nj],
                                      big1[:, k, t * N:(t + 1) * N], start=(k == 0), stop=(k == CS - 1))
                        last.then_inc((gate_done, up_done)[s], 1)
                pe.wait_ge(hT_ready, (count + 1) * NT)

            def down(nj, jb, k2):
                pair, count = k2 + (jb * PAIRS + CS), k2 + jb * (CS // 2)
                for s in range(2):
                    pe.wait_ge(w_ready[s], pair + 1)
                    for t in range(NT):
                        for k in range(CS):
                            last = mm(ps[:, 4 * s + t, :], w_rep[0:nj, s, k, :],
                                      big2[0:nj, k, t * N:(t + 1) * N], start=(k == 0), stop=(k == CS - 1))
                        last.then_inc(down_done, 1)
                pe.wait_ge(y_added, (count + 1) * (2 * NT))

            for jb, (_, nj) in enumerate(JBLOCKS):
                with pe.Fori(0, CS) as e:
                    gate_up(nj, jb, e)
                with pe.Fori(0, CS // 2) as k2:
                    down(nj, jb, k2)

            with pe.Fori(0, SB) as k:
                pe.wait_ge(y_blk_ready, k + 1)
                for e in range(CS):
                    last = nc.tensor.transpose(ps[:, e // 4, (e % 4) * P:(e % 4 + 1) * P],
                                               y_blk[:, e, :], id_sb[:, :])
                last.then_inc(y_nat_done, 1)
                pe.wait_ge(out_ready, k + 1)

        @block.scalar
        def _(act):
            for dst, src in ((id_sb, ident), (rot_sb, rot)):
                act.dma_start(dst[:, :], src).then_inc(const_in, 16)
            act.dma_start(cos_sb, cos).then_inc(const_in, 16)
            act.dma_start(sin_sb, sin).then_inc(const_in, 16)
            act.dma_start(rtmp[:, 0, 0:P], mask).then_inc(const_in, 16)
            xT_v = xT.rearrange("(k p) s -> p k s", p=P)
            wT_v = [w.rearrange("(k p) d -> p k d", p=P) for w in (wqT, wkT, wvT)]
            for k in range(KT):
                act.dma_start(big1[:, k, :], xT_v[:, k, :]).then_inc(xT_in, 16)

            def attention(i):
                for m in range(3):
                    act.wait_ge(proj_done, i * 3 + (m + 1))
                    act.copy(qkv[:, m, :].rearrange("p (h t) -> p h t", h=2),
                             ps[:, 2 * m:2 * m + 2, :]).then_inc(qkv_copied, 1)
                act.wait_ge(vT_done, i + 1)
                act.copy(v_nat.rearrange("p (h s) d -> p h (s d)", h=2), ps[:, 2:4, :]).then_inc(v_ready, 1)

                def exponent(n):
                    L = (n % TB + 1) * P
                    act.wait_ge(negmax_done, i * STEPS + (n + 1))
                    if n >= 2:
                        act.wait_ge(probsT_done, i * STEPS + (n - 1))
                    src = ps[:, 4 * (n % 2):4 * (n % 2) + 2, :].rearrange("p h t -> p (h t)")
                    act.activation(probs[:, n % 2, 0:L], src[:, 0:L], ACT.Exp, bias=negmax[:, n % 2:n % 2 + 1],
                                   scale=SCALE, accum_out=rowsum[:, n % 2:n % 2 + 1]).then_inc(exp_done, 1)

                def copy_turned(n):
                    tb = n % TB
                    act.wait_ge(probsT_done, i * STEPS + (n + 1))
                    if n >= 2:
                        act.wait_ge(pv_done, i * STEPS + (n - 1))
                    src = ps[:, 2:4, :].rearrange("p h t -> p (h t)")
                    dst = probsT[:, n % 2, :, :].rearrange("p s t -> p (s t)")
                    act.copy(dst[:, 0:(tb + 1) * P], src[:, 0:(tb + 1) * P]).then_inc(probsT_copied, 1)

                for n in range(STEPS + 1):
                    if n < STEPS:
                        exponent(n)
                    if n >= 1:
                        copy_turned(n - 1)
                act.wait_ge(pv_done, i * STEPS + STEPS)

            with act.Fori(0, NG) as g:
                for m in range(3):
                    act.dma_start(w_sb[:, m, :, :], wT_v[m][:, :, bass.ds(g * P, P)]).then_inc(w_in, 16)
                with act.Fori(0, B) as b:
                    attention(g * B + b)

            act.wait_ge(oT_ready, NG * B)
            act.dma_start(wo_sb, woT.rearrange("(g p) d -> p g d", p=P)).then_inc(wo_in, 16)
            act.wait_ge(eps_ready, 1)

            def layernorm_std(var_sem, std_sem, k):
                act.wait_ge(var_sem, k + 1)
                act.activation(std, meanvar[:, 1:2], ACT.Sqrt, bias=eps_sb, scale=1.0).then_inc(std_sem, 1)

            with act.Fori(0, SB) as k:
                act.dma_start(x_blk, x_nat[bass.ds(k * P, P), :]).then_inc(x_in, 16)
                act.copy(o_blk, big2[:, :, bass.ds(k * P, P)]).then_inc(o_blk_ready, 1)
                layernorm_std(var_ready, std_ready, k)
                act.wait_ge(x1T_done, k + 1)
                act.copy(big1[:, :, bass.ds(k * P, P)],
                         ps[:, 2:4, :].rearrange("p h (e s) -> p (h e) s", e=4)).then_inc(x1T_ready, 1)

            def load_unit(rows, cols, pair, s):
                act.wait_ge(stored[s], (pair + 1) * 16)
                act.dma_start(w_raw[0:rows, s, 0:cols, :].rearrange("p n e -> p (n e)"),
                              units[pair, s, 0:rows, 0:cols * CS]).then_inc(w_loaded[s], 16)

            def repack(rows, cols, pair, s):
                act.wait_ge(w_loaded[s], (pair + 1) * 16)
                act.copy(w_rep[0:rows, s, :, 0:cols],
                         w_raw[0:rows, s, 0:cols, :].rearrange("p n e -> p e n")).then_inc(w_ready[s], 1)

            def gate_up(nj, jb, e):
                pair, count = e + jb * PAIRS, e + jb * CS
                for s in range(2):
                    load_unit(P, nj, pair, s)
                for s in range(2):
                    repack(P, nj, pair, s)
                for t in range(NT):
                    act.wait_ge(gate_done, count * NT + (t + 1))
                    if t >= 2:
                        act.wait_ge(hT_ready, count * NT + (t - 1))
                    act.activation(silu[0:nj, t % 2, :], ps[0:nj, t, :], ACT.Silu).then_inc(silu_ready, 1)
                act.wait_ge(hT_ready, count * NT + NT)

            def down(nj, jb, k2):
                pair, count = k2 + (jb * PAIRS + CS), k2 + jb * (CS // 2)
                for s in range(2):
                    load_unit(nj, P, pair, s)
                    if jb:
                        act.dma_start(y_sb[:, s, :], yT_dram[k2 * 2 + s]).then_inc(y_in[s], 16)
                for s in range(2):
                    repack(nj, P, pair, s)
                for s in range(2):
                    act.wait_ge(y_added, count * (2 * NT) + (s + 1) * NT)
                    if jb < len(JBLOCKS) - 1:
                        act.dma_start(yT_dram[k2 * 2 + s], y_sb[:, s, :]).then_inc(y_out[s], 16)
                if jb < len(JBLOCKS) - 1:
                    for s in range(2):
                        act.wait_ge(y_out[s], (count + 1) * 16)

            for jb, (_, nj) in enumerate(JBLOCKS):
                with act.Fori(0, CS) as e:
                    gate_up(nj, jb, e)
                with act.Fori(0, CS // 2) as k2:
                    down(nj, jb, k2)

            with act.Fori(0, SB) as k:
                act.copy(y_blk, big1[:, :, bass.ds(k * P, P)]).then_inc(y_blk_ready, 1)
                layernorm_std(var2_ready, std2_ready, k)
                act.wait_ge(out_ready, k + 1)
                act.dma_start(out[bass.ds(k * P, P), :], out_blk).then_inc(out_stored, 16)
                act.wait_ge(out_stored, k * 16 + 16)

        @block.vector
        def _(dve):
            dve.memset(eps_sb, EPS).then_inc(eps_ready, 1)
            dve.wait_ge(const_in, 16 * 5)
            dve.tensor_copy(mask_sb[:, :], rtmp[:, 0, 0:P]).then_inc(mask_ready, 1)
            dve.tensor_copy(idb_sb[:, :], id_sb[:, :]).then_inc(mask_ready, 1)
            dve.wait_ge(mask_ready, 2)

            def attention(i, g, b):
                two = lambda a: a.rearrange("p (h t) -> p h t", h=2)
                for m in range(2):
                    bank = 6 if m == 0 else 0
                    dve.wait_ge(rot_done, i * 2 + (m + 1))
                    dve.tensor_tensor(two(qkv[:, m, :]), two(qkv[:, m, :]), two(cos_sb), ALU.mult).then_inc(rope_step, 1)
                    dve.tensor_tensor(two(rtmp[:, m, :]), ps[:, bank:bank + 2, :], two(sin_sb), ALU.mult).then_inc(rope_step, 1)
                    dve.wait_ge(rope_step, i * 4 + (2 * m + 2))
                    dve.tensor_tensor(qkv[:, m, :], qkv[:, m, :], rtmp[:, m, :], ALU.add).then_inc(qk_ready, 1)

                def row_max(n):
                    L = (n % TB + 1) * P
                    o = n % 2
                    dve.wait_ge(scores_done, i * STEPS + (n + 1))
                    src = ps[:, 4 * o:4 * o + 2, :].rearrange("p h t -> p (h t)")
                    dve.reduce_max(rowmax[:, o:o + 1], src[:, 0:L], AX.X).then_inc(max_done, 1)
                    dve.wait_ge(max_done, i * STEPS + (n + 1))
                    dve.tensor_scalar(negmax[:, o:o + 1], rowmax[:, o:o + 1], -SCALE, None, ALU.mult).then_inc(negmax_done, 1)

                def normalise(n):
                    L = (n % TB + 1) * P
                    o = n % 2
                    dve.wait_ge(exp_done, i * STEPS + (n + 1))
                    dve.reciprocal(rinv[:, o:o + 1], rowsum[:, o:o + 1]).then_inc(rinv_done, 1)
                    dve.wait_ge(rinv_done, i * STEPS + (n + 1))
                    dve.tensor_scalar(probs[:, o, 0:L], probs[:, o, 0:L], rinv[:, o:o + 1], None,
                                      ALU.mult).then_inc(probs_ready, 1)

                for n in range(STEPS + 1):
                    if n < STEPS:
                        row_max(n)
                    if n >= 1:
                        normalise(n - 1)
                dve.wait_ge(pv_done, i * STEPS + STEPS)
                dve.tensor_copy(two(big2[:, g, bass.ds(b * T, T)]), ps[:, 6:8, :]).then_inc(oT_ready, 1)

            with dve.Fori(0, NG) as g:
                with dve.Fori(0, B) as b:
                    attention(g * B + b, g, b)

            def layernorm(src, k, step, var_sem, std_sem, write):
                for h in range(2):
                    dve.bn_stats(stats[:, h, :], src[:, h, :]).then_inc(step, 1)
                dve.wait_ge(step, k * 3 + 2)
                dve.sem_inc(dve_passed, 1)
                dve.bn_aggr(meanvar, stats.rearrange("p n k -> p (n k)")).then_inc(var_sem, 1)
                dve.wait_ge(std_sem, k + 1)
                dve.reciprocal(rstd, std).then_inc(step, 1)
                dve.wait_ge(step, k * 3 + 3)
                write()

            with dve.Fori(0, SB) as k:
                dve.wait_ge(wo_done, k + 1)
                dve.wait_ge(x_in, k * 16 + 16)
                x_v = x_blk.rearrange("p (h d) -> p h d", h=2)
                dve.tensor_tensor(x_v, ps[:, 0:2, :], x_v, ALU.add).then_inc(sum_ready, 1)
                dve.wait_ge(sum_ready, k + 1)
                layernorm(x_v, k, ln_step, var_ready, std_ready,
                          lambda: dve.tensor_scalar(x1_blk, x_blk, meanvar[:, 0:1], rstd, ALU.subtract,
                                                    ALU.mult).then_inc(x1_ready, 1))
                dve.wait_ge(x1T_ready, k + 1)

            def gate_up(nj, jb, e):
                count = e + jb * CS
                for t in range(NT):
                    dve.wait_ge(silu_ready, count * NT + (t + 1))
                    dve.wait_ge(up_done, count * NT + (t + 1))
                    dve.tensor_tensor(big2[0:nj, e, t * N:(t + 1) * N], silu[0:nj, t % 2, :], ps[0:nj, 4 + t, :],
                                      ALU.mult).then_inc(hT_ready, 1)

            def down(nj, jb, k2):
                count = k2 + jb * (CS // 2)
                for s in range(2):
                    if jb:
                        dve.wait_ge(y_in[s], (k2 + (jb - 1) * (CS // 2)) * 16 + 16)
                    for t in range(NT):
                        cols = slice(t * N, (t + 1) * N)
                        dve.wait_ge(down_done, count * (2 * NT) + (s * NT + t + 1))
                        before = big1[:, k2 * 2 + s, cols] if jb == 0 else y_sb[:, s, cols]
                        after = big1[:, k2 * 2 + s, cols] if jb == len(JBLOCKS) - 1 else y_sb[:, s, cols]
                        dve.tensor_tensor(after, ps[:, 4 * s + t, :], before, ALU.add).then_inc(y_added, 1)

            for jb, (_, nj) in enumerate(JBLOCKS):
                with dve.Fori(0, CS) as e:
                    gate_up(nj, jb, e)
                with dve.Fori(0, CS // 2) as k2:
                    down(nj, jb, k2)

            with dve.Fori(0, SB) as k:
                dve.wait_ge(y_nat_done, k + 1)
                src = ps[:, 0:2, :]
                out_v = out_blk.rearrange("p (c e) -> p e c", e=CS)
                layernorm(src, k, ln2_step, var2_ready, std2_ready,
                          lambda: dve.tensor_scalar(out_v, src.rearrange("p h (e c) -> p (h e) c", e=4),
                                                    meanvar[:, 0:1], rstd, ALU.subtract,
                                                    ALU.mult).then_inc(out_ready, 1))
                dve.wait_ge(out_stored, k * 16 + 16)


def rope_tables():
    pos = np.arange(T, dtype=np.float32)
    thetas = (np.float32(1.0) / np.float32(10000.0) ** (np.arange(0, HD, 2, dtype=np.float32) / np.float32(HD))).astype(np.float32)
    angle = np.outer(pos, thetas).astype(np.float32)
    angle = np.concatenate([angle, angle], axis=-1)
    sign = np.where(np.arange(HD) < HD // 2, -1.0, 1.0).astype(np.float32)
    cos = np.tile(np.cos(angle).T, (HG, 1)).astype(np.float32)
    sin = np.tile((np.sin(angle) * sign).T, (HG, 1)).astype(np.float32)
    return cos, sin


def constants():
    d = np.arange(P)
    swap = (d // HD) * HD + (d + HD // 2) % HD
    rot = np.zeros((P, P), np.float32)
    rot[swap, d] = 1.0
    mask = np.where(d[None, :] > d[:, None], MASKED, 0.0)
    return np.eye(P, dtype=np.float32), rot, mask.astype(np.float32)


def lay_out_indices(gate, up, down):
    gate, up = (a.reshape(NJ, CS, C // CS).transpose(1, 2, 0) for a in (gate, up))
    down = down.reshape(P, CS, NJ).transpose(1, 2, 0)
    idx = np.zeros((NPAIR, 2, P, P), gate.dtype)
    for jb, (j0, nj) in enumerate(JBLOCKS):
        for e in range(CS):
            idx[jb * PAIRS + e, 0, :, :nj] = gate[e, :, j0:j0 + nj]
            idx[jb * PAIRS + e, 1, :, :nj] = up[e, :, j0:j0 + nj]
            idx[jb * PAIRS + CS + e // 2, e % 2, :nj, :] = down[e, j0:j0 + nj, :]
    return idx


def kernel(**inputs):
    import concourse.bacc as _bacc
    from concourse.bass_utils import run_bass_kernel_spmd as _run

    a = {k: np.asarray(v) for k, v in inputs.items()}
    x = a["L0_attn_x"].reshape(S, C)
    cos, sin = rope_tables()
    ident, rot, mask = constants()
    data = {
        "x": x, "xT": x.T, "wqT": a["L0_attn_wq"].T, "wkT": a["L0_attn_wk"].T, "wvT": a["L0_attn_wv"].T,
        "woT": a["L0_attn_wo"].T, "codebook": a["L0_ffn_codebook"],
        "idx": lay_out_indices(a["L0_ffn_idx_gate"], a["L0_ffn_idx_up"], a["L0_ffn_idx_down"]),
        "cos": cos, "sin": sin, "rot": rot, "ident": ident, "mask": mask,
    }
    nc = _bacc.Bacc("TRN2", target_bir_lowering=False, num_devices=1)
    arrays, args = {}, []
    for name, v in data.items():
        v = np.ascontiguousarray(v)
        arrays[f"in_{name}_dram"] = v
        args.append(nc.dram_tensor(f"in_{name}_dram", v.shape, mybir.dt.from_np(v.dtype), kind="ExternalInput").ap())
    out = nc.dram_tensor("out_0_dram", (S, C), F32, kind="ExternalOutput").ap()
    seq_post_ln_layer(nc, *args, out)
    r = _run(nc, [arrays], core_ids=[0])
    return r.results[0]["out_0_dram"].reshape(B, T, C)
```
